# Optimizing a Trainium2 kernel written in Bass

```python
import numpy as np
import jax
import jax.numpy as jnp

def _softmax(x, axis=-1):
    return jax.nn.softmax(x, axis=axis)

def _gelu(x):
    return jax.nn.gelu(x, approximate=True)

def _silu(x):
    return jax.nn.silu(x)

def _sigmoid(x):
    return jax.nn.sigmoid(x)

def _layernorm(x, axis=-1, eps=1e-05):
    m = jnp.mean(x, axis=axis, keepdims=True)
    v = jnp.var(x, axis=axis, keepdims=True)
    return (x - m) / jnp.sqrt(v + eps)

def _scatter_add(tgt, idx, src, axis=0):
    return tgt.at[idx].add(src)

def _segment_sum(src, seg, n):
    return jax.ops.segment_sum(src, seg, n)
kernel_name = 'mk_dlrm_tower_d1_rec_r8_6635b7'

def setup_inputs(seed: int=0):
    np.random.seed(seed)
    _w = jnp.asarray

    def _rec_inputs():
        import jax
        import jax.numpy as jnp
        _tk = jax.random.key(seed)
        ids = jnp.stack([jax.random.randint(jax.random.fold_in(_tk, 200 + f), (2048,), 0, v, jnp.int32) for f, v in enumerate([125000, 1000, 12500, 12500, 12500, 1000, 12500, 1250, 1000, 12500, 1250, 1250, 1000, 1000, 1000, 1250, 12500, 12500, 12500, 1250, 1250, 1000, 1250, 1250, 1000, 1000])], axis=1)
        tbl_0 = 0.05 * jax.random.normal(jax.random.fold_in(_tk, 500 + 0), (125000, 128), jnp.float32)
        tbl_1 = 0.05 * jax.random.normal(jax.random.fold_in(_tk, 500 + 1), (1000, 128), jnp.float32)
        tbl_2 = 0.05 * jax.random.normal(jax.random.fold_in(_tk, 500 + 2), (12500, 128), jnp.float32)
        tbl_3 = 0.05 * jax.random.normal(jax.random.fold_in(_tk, 500 + 3), (12500, 128), jnp.float32)
        tbl_4 = 0.05 * jax.random.normal(jax.random.fold_in(_tk, 500 + 4), (12500, 128), jnp.float32)
        tbl_5 = 0.05 * jax.random.normal(jax.random.fold_in(_tk, 500 + 5), (1000, 128), jnp.float32)
        tbl_6 = 0.05 * jax.random.normal(jax.random.fold_in(_tk, 500 + 6), (12500, 128), jnp.float32)
        tbl_7 = 0.05 * jax.random.normal(jax.random.fold_in(_tk, 500 + 7), (1250, 128), jnp.float32)
        tbl_8 = 0.05 * jax.random.normal(jax.random.fold_in(_tk, 500 + 8), (1000, 128), jnp.float32)
        tbl_9 = 0.05 * jax.random.normal(jax.random.fold_in(_tk, 500 + 9), (12500, 128), jnp.float32)
        tbl_10 = 0.05 * jax.random.normal(jax.random.fold_in(_tk, 500 + 10), (1250, 128), jnp.float32)
        tbl_11 = 0.05 * jax.random.normal(jax.random.fold_in(_tk, 500 + 11), (1250, 128), jnp.float32)
        tbl_12 = 0.05 * jax.random.normal(jax.random.fold_in(_tk, 500 + 12), (1000, 128), jnp.float32)
        tbl_13 = 0.05 * jax.random.normal(jax.random.fold_in(_tk, 500 + 13), (1000, 128), jnp.float32)
        tbl_14 = 0.05 * jax.random.normal(jax.random.fold_in(_tk, 500 + 14), (1000, 128), jnp.float32)
        tbl_15 = 0.05 * jax.random.normal(jax.random.fold_in(_tk, 500 + 15), (1250, 128), jnp.float32)
        tbl_16 = 0.05 * jax.random.normal(jax.random.fold_in(_tk, 500 + 16), (12500, 128), jnp.float32)
        tbl_17 = 0.05 * jax.random.normal(jax.random.fold_in(_tk, 500 + 17), (12500, 128), jnp.float32)
        tbl_18 = 0.05 * jax.random.normal(jax.random.fold_in(_tk, 500 + 18), (12500, 128), jnp.float32)
        tbl_19 = 0.05 * jax.random.normal(jax.random.fold_in(_tk, 500 + 19), (1250, 128), jnp.float32)
        tbl_20 = 0.05 * jax.random.normal(jax.random.fold_in(_tk, 500 + 20), (1250, 128), jnp.float32)
        tbl_21 = 0.05 * jax.random.normal(jax.random.fold_in(_tk, 500 + 21), (1000, 128), jnp.float32)
        tbl_22 = 0.05 * jax.random.normal(jax.random.fold_in(_tk, 500 + 22), (1250, 128), jnp.float32)
        tbl_23 = 0.05 * jax.random.normal(jax.random.fold_in(_tk, 500 + 23), (1250, 128), jnp.float32)
        tbl_24 = 0.05 * jax.random.normal(jax.random.fold_in(_tk, 500 + 24), (1000, 128), jnp.float32)
        tbl_25 = 0.05 * jax.random.normal(jax.random.fold_in(_tk, 500 + 25), (1000, 128), jnp.float32)
        _rk = jax.random.fold_in(_tk, 7)
        r_dense_x = -0.000514642 + 1.00011 * jax.random.normal(jax.random.fold_in(_rk, 101), (2048, 128), jnp.float32)
        W_top1 = 0.0456912 * jax.random.normal(jax.random.fold_in(_tk, 801), (479, 512), jnp.float32)
        W_top2 = 0.0441942 * jax.random.normal(jax.random.fold_in(_tk, 802), (512, 256), jnp.float32)
        W_top3 = 0.0625 * jax.random.normal(jax.random.fold_in(_tk, 803), (256, 1), jnp.float32)
        b_top1 = jnp.zeros((512,), jnp.float32)
        b_top2 = jnp.zeros((256,), jnp.float32)
        return (r_dense_x, ids, tbl_0, tbl_1, tbl_2, tbl_3, tbl_4, tbl_5, tbl_6, tbl_7, tbl_8, tbl_9, tbl_10, tbl_11, tbl_12, tbl_13, tbl_14, tbl_15, tbl_16, tbl_17, tbl_18, tbl_19, tbl_20, tbl_21, tbl_22, tbl_23, tbl_24, tbl_25, W_top1, b_top1, W_top2, b_top2, W_top3)
    r_dense_x, ids, tbl_0, tbl_1, tbl_2, tbl_3, tbl_4, tbl_5, tbl_6, tbl_7, tbl_8, tbl_9, tbl_10, tbl_11, tbl_12, tbl_13, tbl_14, tbl_15, tbl_16, tbl_17, tbl_18, tbl_19, tbl_20, tbl_21, tbl_22, tbl_23, tbl_24, tbl_25, W_top1, b_top1, W_top2, b_top2, W_top3 = _rec_inputs()

    def _L0_rec_setup():
        import jax, jax.numpy as jnp
        import numpy as np
        F = 26
        D = 128
        B = 2048
        _TRIU_I, _TRIU_J = np.triu_indices(F + 1, k=1)
        _TRIU_I = jnp.asarray(_TRIU_I)
        _TRIU_J = jnp.asarray(_TRIU_J)
        key = jax.random.key(seed)
        k1, k2 = jax.random.split(key)
        sparse_x = jax.random.normal(k1, (B, F, D), dtype=jnp.float32)
        dense_x = jax.random.normal(k2, (B, D), dtype=jnp.float32)
        return {'sparse_x': sparse_x, 'dense_x': dense_x}
    _L0_rec_all = _L0_rec_setup()
    _L0_rec_in = {k: v for k, v in _L0_rec_all.items() if k in ()}
    del _L0_rec_all
    return {'r_dense_x': r_dense_x, 'ids': ids, 'tbl_0': tbl_0, 'tbl_1': tbl_1, 'tbl_2': tbl_2, 'tbl_3': tbl_3, 'tbl_4': tbl_4, 'tbl_5': tbl_5, 'tbl_6': tbl_6, 'tbl_7': tbl_7, 'tbl_8': tbl_8, 'tbl_9': tbl_9, 'tbl_10': tbl_10, 'tbl_11': tbl_11, 'tbl_12': tbl_12, 'tbl_13': tbl_13, 'tbl_14': tbl_14, 'tbl_15': tbl_15, 'tbl_16': tbl_16, 'tbl_17': tbl_17, 'tbl_18': tbl_18, 'tbl_19': tbl_19, 'tbl_20': tbl_20, 'tbl_21': tbl_21, 'tbl_22': tbl_22, 'tbl_23': tbl_23, 'tbl_24': tbl_24, 'tbl_25': tbl_25, 'W_top1': W_top1, 'b_top1': b_top1, 'W_top2': W_top2, 'b_top2': b_top2, 'W_top3': W_top3}

def reference(r_dense_x, ids, tbl_0, tbl_1, tbl_2, tbl_3, tbl_4, tbl_5, tbl_6, tbl_7, tbl_8, tbl_9, tbl_10, tbl_11, tbl_12, tbl_13, tbl_14, tbl_15, tbl_16, tbl_17, tbl_18, tbl_19, tbl_20, tbl_21, tbl_22, tbl_23, tbl_24, tbl_25, W_top1, b_top1, W_top2, b_top2, W_top3):
    import jax
    import jax.numpy as jnp

    def _L0_rec_ref(sparse_x, dense_x):
        import jax, jax.numpy as jnp
        import numpy as np
        F = 26
        D = 128
        B = 2048
        _TRIU_I, _TRIU_J = np.triu_indices(F + 1, k=1)
        _TRIU_I = jnp.asarray(_TRIU_I)
        _TRIU_J = jnp.asarray(_TRIU_J)
        combined = jnp.concatenate([sparse_x, dense_x[:, None, :]], axis=1)
        interact = jnp.einsum('bfd,bgd->bfg', combined, combined)
        return interact[:, _TRIU_I, _TRIU_J]
    e = jnp.stack([tbl_0[ids[:, 0]], tbl_1[ids[:, 1]], tbl_2[ids[:, 2]], tbl_3[ids[:, 3]], tbl_4[ids[:, 4]], tbl_5[ids[:, 5]], tbl_6[ids[:, 6]], tbl_7[ids[:, 7]], tbl_8[ids[:, 8]], tbl_9[ids[:, 9]], tbl_10[ids[:, 10]], tbl_11[ids[:, 11]], tbl_12[ids[:, 12]], tbl_13[ids[:, 13]], tbl_14[ids[:, 14]], tbl_15[ids[:, 15]], tbl_16[ids[:, 16]], tbl_17[ids[:, 17]], tbl_18[ids[:, 18]], tbl_19[ids[:, 19]], tbl_20[ids[:, 20]], tbl_21[ids[:, 21]], tbl_22[ids[:, 22]], tbl_23[ids[:, 23]], tbl_24[ids[:, 24]], tbl_25[ids[:, 25]]], axis=1)
    z = _L0_rec_ref(e, r_dense_x)
    z = z.reshape(z.shape[0], -1)
    h = jnp.concatenate([z, r_dense_x], axis=1)
    h = jnp.maximum(h @ W_top1 + b_top1, 0.0)
    h = jnp.maximum(h @ W_top2 + b_top2, 0.0)
    y = h @ W_top3
    return y

_drawn_inputs = setup_inputs


def setup_inputs(seed=0):
    import zlib

    import numpy as np

    out = dict(_drawn_inputs(seed))
    spreads = {'b_top1': (0.0, 0.1), 'b_top2': (0.0, 0.1)}
    factors = {}
    for name, (base, spread) in spreads.items():
        noise = np.random.default_rng([zlib.crc32(name.encode()), seed]).standard_normal(out[name].shape)
        drawn = base * np.exp(spread * noise) if base else spread * noise
        out[name] = jnp.asarray(drawn.astype(out[name].dtype))
    for name, factor in factors.items():
        out[name] = (out[name] * factor).astype(out[name].dtype)
    return out
```

```python
from contextlib import ExitStack

import numpy as np

import concourse.bass as bass
from concourse import mybir

P = 128
B = 2048
D = 128
NF = 27
DENSE = 26
QUAD = 32
SPG = P // QUAD
GROUPS = P // SPG
TILES = B // P
PAIRS = B // (2 * P)
S2 = 2 * P

ONEHOT = [1, 5, 8, 12, 13, 14]
GATHERED = [f for f in range(26) if f not in ONEHOT]
COLUMN_OF = GATHERED + [DENSE] + ONEHOT
NG = len(GATHERED)
NO = len(ONEHOT)
OH_ROWS = 1000
OH_K = 8
OH_P = OH_ROWS // OH_K
OH_FILLS = NO // 2
RING = 2 * OH_K
TCH = 4
T_FILLS = (NG + 1 + TCH - 1) // TCH
FRONT = 2 * T_FILLS + OH_FILLS
GCHUNKS = 4
CG = GROUPS // GCHUNKS
BACK = 6

NPAIR = NF * (NF - 1) // 2
HALF = (NF - 1) // 2
TOP = NF - HALF
PITCH = NF + HALF
ZK = 3
ZP = NPAIR // ZK
H1, H2 = 512, 256

F32 = mybir.dt.float32
F32R = mybir.dt.float32r
I32 = mybir.dt.int32
ALU = mybir.AluOpType
ACT = mybir.ActivationFunctionType


def pair_order():
    return [(g, (g + k) % NF) for g in range(NF) for k in range(1, HALF + 1)]


def top1_row_order():
    first = {}
    for i in range(NF):
        for j in range(i + 1, NF):
            first[(i, j)] = len(first)
    rows = []
    for a, b in pair_order():
        i, j = sorted((COLUMN_OF[a], COLUMN_OF[b]))
        rows.append(first[(i, j)])
    return rows + list(range(NPAIR, NPAIR + D))


def build(nc, dense, ids, ids_t, w1, b1, w2, b2, w3, out, tables):
    with ExitStack() as ctx:
        def sb(name, shape, dt=F32):
            return ctx.enter_context(nc.sbuf_tensor(name, shape, dt))

        def psum(name, shape):
            return ctx.enter_context(nc.psum_tensor(name, shape, F32))

        def sem(name):
            return ctx.enter_context(nc.semaphore(name))

        ct = sb("ct", [P, 4, GROUPS, SPG, QUAD])
        gat = sb("gat", [P, 2, NG + 1, D])
        idx = sb("idx", [P, 2, 26], I32)
        idb = sb("idb", [P, NO, S2], I32)
        tab_hi = sb("tab_hi", [P, NO, OH_K, D], F32R)
        tab_lo = sb("tab_lo", [P, NO, OH_K, D], F32R)
        ring = sb("ring", [P, RING, S2], F32R)
        rowid_i = sb("rowid_i", [P, OH_K], I32)
        rowid = sb("rowid", [P, OH_K])
        ident = sb("ident", [P, P])
        z1 = sb("z1", [P, GROUPS, NF])
        z2 = sb("z2", [P, NF, PITCH])
        zc = sb("zc", [P, 2, NPAIR])
        zt = sb("zt", [P, 2, ZK, S2])
        dt = sb("dt", [P, 2, S2])
        w1z = sb("w1z", [P, ZK, H1])
        w1d = sb("w1d", [P, H1])
        w2s = sb("w2s", [P, H1 // P, H2])
        w3s = sb("w3s", [P, H2 // P])
        b1s = sb("b1s", [P, H1 // P])
        b2s = sb("b2s", [P, H2 // P])
        h1 = sb("h1", [P, H1 // P, S2])
        h2 = sb("h2", [P, H2 // P, S2])
        yrow = sb("yrow", [1, 2, S2])

        front = psum("front", [P, 2, 512])
        gram = psum("gram", [P, 2, CG, P])
        back = psum("back", [P, 2, 512])

        ids_in = [sem(f"ids_in{i}") for i in range(2)]
        dense_in = [sem(f"dense_in{i}") for i in range(2)]
        gathered = [sem(f"gathered{i}") for i in range(2)]
        idb_in = [sem(f"idb_in{i}") for i in range(OH_FILLS)]
        table_in = [sem(f"table_in{i}") for i in range(NO)]
        weights_in = sem("weights_in")
        rowid_ready = sem("rowid_ready")
        ident_zeroed = sem("ident_zeroed")
        ident_ready = sem("ident_ready")
        const_cast = sem("const_cast")
        pads_ready = sem("pads_ready")
        hi_ready = sem("hi_ready")
        lo_ready = sem("lo_ready")
        transposed = sem("transposed")
        front_free = sem("front_free")
        built = sem("built")
        used = sem("used")
        gram_done = sem("gram_done")
        gram_act = sem("gram_act")
        gram_dve = sem("gram_dve")
        z1_turned = sem("z1_turned")
        z2_wrapped = sem("z2_wrapped")
        pairs_ready = sem("pairs_ready")
        back_done = sem("back_done")
        back_free = sem("back_free")
        y_out = sem("y_out")

        def front_index(p, k):
            return OH_FILLS + FRONT * p + k

        def back_index(p, k):
            return 1 + BACK * (p - 1) + k

        def front_bank(par, k):
            return front_index(par, k) % 2

        def back_bank(k):
            return (1 + k) % 2

        def raw_table(o):
            flat = ct[:, 2:4, :, :, :].rearrange("p s g j f -> p (s g j f)")
            return flat[0:OH_P, o * OH_K * D:(o + 1) * OH_K * D]

        def front_fills(last_pair):
            order = []
            for u in range(2):
                order += [("T", u, c) for c in range(T_FILLS)]
            if last_pair:
                return order
            half = T_FILLS // 2
            at = [half, T_FILLS, 2 * T_FILLS]
            for n, a in enumerate(at[:OH_FILLS]):
                order.insert(a + n, ("O", None, n))
            return order

        def run_pairs(eng, body):
            body(0, 0, False)
            with eng.Fori(0, (PAIRS - 2) // 2) as i:
                body(2 * i + 1, 1, False)
                body(2 * i + 2, 0, False)
            body(PAIRS - 1, (PAIRS - 1) % 2, True)

        block = ctx.enter_context(nc.Block())

        @block.sync
        def _(sp):
            def load_ids(t, slot):
                sp.dma_start(idx[:, slot, :], ids[bass.ds(t * P, P), :]).then_inc(ids_in[slot], 16)

            def load_dense(t, slot):
                sp.dma_start(gat[:, slot, NG, :], dense[bass.ds(t * P, P), :]).then_inc(dense_in[slot], 16)

            def load_idb(p, n):
                src = ids_t[2 * n:2 * n + 2, bass.ds(p * S2, S2)].unsqueeze(0).to_broadcast([P, 2, S2])
                sp.dma_start(idb[:, 2 * n:2 * n + 2, :], src).then_inc(idb_in[n], 16)

            for t in range(2):
                load_ids(t, t)
            load_idb(0, 0)
            for o in range(NO):
                sp.dma_start(raw_table(o), tables[ONEHOT[o]].rearrange("(p k) d -> p (k d)", k=OH_K)
                             ).then_inc(table_in[o], 16)
            for n in range(1, OH_FILLS):
                load_idb(0, n)
            for t in range(2):
                load_dense(t, t)
            sp.dma_start(w1z[0:ZP, :, :], w1[0:NPAIR, :].rearrange("(k p) n -> p k n", p=ZP)).then_inc(weights_in, 16)
            sp.dma_start(w1d[:, :], w1[NPAIR:NPAIR + D, :]).then_inc(weights_in, 16)
            sp.dma_start(w2s[:, :, :], w2.rearrange("(k p) n -> p k n", p=P)).then_inc(weights_in, 16)
            with nc.allow_non_contiguous_dma(reason="small vectors, one element per partition"):
                sp.dma_start(w3s[:, :], w3.rearrange("(k p) n -> p (k n)", p=P)).then_inc(weights_in, 16)
                sp.dma_start(b1s[:, :], b1.rearrange("(k p) -> p k", p=P)).then_inc(weights_in, 16)
                sp.dma_start(b2s[:, :], b2.rearrange("(k p) -> p k", p=P)).then_inc(weights_in, 16)

            def next_idb(p, n):
                sp.wait_ge(built, RING * (OH_FILLS * p + n + 1))
                load_idb(p + 1, n)

            def pair(p, par, last):
                for u in range(2):
                    t = 2 * p + u
                    if not (isinstance(p, int) and p == 0):
                        sp.wait_ge(gathered[u], 16 * NG * p)
                        load_ids(t, u)
                        sp.wait_ge(transposed, T_FILLS * (t - 1))
                        load_dense(t, u)
                    if not last:
                        for n in ((0, 1) if u == 0 else range(2, OH_FILLS)):
                            next_idb(p, n)

            run_pairs(sp, pair)

        @block.gpsimd
        def _(pool):
            nc.gpsimd.iota(rowid_i[:, :], pattern=[[1, OH_K]], base=0, channel_multiplier=OH_K).then_inc(rowid_ready, 1)
            nc.gpsimd.memset(ident[:, :], 0.0).then_inc(ident_zeroed, 1)
            pool.wait_ge(ident_zeroed, 1)
            nc.gpsimd.affine_select(out=ident[:, :], in_=ident[:, :], compare_op=ALU.not_equal, fill=1.0, base=0,
                                    pattern=[[-1, P]], channel_multiplier=1).then_inc(ident_ready, 1)

            def pair(p, par, last):
                for u in range(2):
                    t = 2 * p + u
                    pool.wait_ge(ids_in[u], 16 * (p + 1))
                    pool.nop(nofuse=True)
                    for i, f in enumerate(GATHERED):
                        if i % TCH == 0 and not (isinstance(p, int) and p == 0):
                            pool.wait_ge(transposed, T_FILLS * (t - 2) + i // TCH + 1)
                            pool.nop(nofuse=True)
                        nc.gpsimd.indirect_dma_start(
                            out=gat[:, u, i, :], out_offset=None, in_=tables[f][:, :],
                            in_offset=bass.IndirectOffsetOnAxis(ap=idx[:, u, f:f + 1], axis=0),
                        ).then_inc(gathered[u], 16)

            run_pairs(pool, pair)

        @block.tensor
        def _(pe):
            def front_wait(p, k):
                pe.wait_ge(front_free, front_index(p, k) - 1)

            def transpose_fill(p, par, k, u, c):
                front_wait(p, k)
                bank = front_bank(par, k)
                cols = range(c * TCH, min((c + 1) * TCH, NG + 1))
                if c == 0:
                    pe.wait_ge(gathered[u], 16 * NG * (p + 1))
                if NG in cols:
                    pe.wait_ge(dense_in[u], 16 * (p + 1))
                for n, col in enumerate(cols):
                    ins = nc.tensor.transpose(front[:, bank, n * P:(n + 1) * P], gat[:, u, col, :], ident[:, :])
                ins.then_inc(transposed, 1)

            def onehot_fill(p, n, bank):
                for a in range(2):
                    for k in range(OH_K):
                        m = a * OH_K + k
                        pe.wait_ge(built, RING * (OH_FILLS * p + n) + m + 1)
                        dst = front[:, bank, a * S2:(a + 1) * S2]
                        nc.tensor.matmul(dst, tab_hi[0:OH_P, 2 * n + a, k, :], ring[0:OH_P, m, :],
                                         start=(k == 0), stop=False)
                        ins = nc.tensor.matmul(dst, tab_lo[0:OH_P, 2 * n + a, k, :], ring[0:OH_P, m, :],
                                               start=False, stop=(k == OH_K - 1))
                        ins.then_inc(used, 1)

            def gram_tile(p, par, u, last):
                t = 2 * p + u
                slot = 2 * par + u
                pe.wait_ge(front_free, front_index(p, front_fills(last).index(("T", u, T_FILLS - 1))) + 1)
                for c in range(GCHUNKS):
                    n = GCHUNKS * t + c
                    if not (isinstance(p, int) and GCHUNKS * (2 * p + u) + c < 2):
                        pe.wait_ge(gram_act, n - 1)
                        pe.wait_ge(gram_dve, n - 1)
                    for i in range(CG):
                        g = c * CG + i
                        ins = nc.tensor.matmul(
                            gram[:, c % 2, i, 0:SPG * (NF)].rearrange("p (j f) -> p j f", j=SPG),
                            ct[:, slot, g, :, :].rearrange("p j f -> p (j f)"),
                            ct[:, slot, g, :, 0:NF], start=True, stop=True)
                    ins.then_inc(gram_done, 1)

            def back_wait(p, k):
                pe.wait_ge(back_free, back_index(p, k) - 1)

            def pair_transposes(t, tpar, index, bank, first=False):
                pe.wait_ge(pairs_ready, t + 1)
                if not first:
                    pe.wait_ge(back_free, index)
                for k in range(ZK):
                    ins = nc.tensor.transpose(back[0:ZP, bank, k * P:(k + 1) * P],
                                              zc[:, tpar, k * ZP:(k + 1) * ZP], ident[:, :])
                ins.then_inc(back_done, 1)

            def layer1(p, q):
                for half in range(2):
                    back_wait(p, 1 + half)
                    if half == 0:
                        pe.wait_ge(back_free, back_index(p, 0) + 1)
                    for n in range(2):
                        m = 2 * half + n
                        dst = back[:, back_bank(1 + half), n * S2:(n + 1) * S2]
                        for k in range(ZK):
                            nc.tensor.matmul(dst, w1z[0:ZP, k, m * P:(m + 1) * P], zt[0:ZP, q, k, :],
                                             start=(k == 0), stop=False)
                        ins = nc.tensor.matmul(dst, w1d[:, m * P:(m + 1) * P], dt[:, q, :], start=False, stop=True)
                    ins.then_inc(back_done, 1)

            def layer2(p):
                pe.wait_ge(back_free, back_index(p, 2) + 1)
                for n in range(H2 // P):
                    dst = back[:, back_bank(3), n * S2:(n + 1) * S2]
                    for k in range(H1 // P):
                        ins = nc.tensor.matmul(dst, w2s[:, k, n * P:(n + 1) * P], h1[:, k, :],
                                               start=(k == 0), stop=(k == H1 // P - 1))
                ins.then_inc(back_done, 1)

            def layer3(p):
                pe.wait_ge(back_free, back_index(p, 3) + 1)
                for k in range(H2 // P):
                    ins = nc.tensor.matmul(back[0:1, back_bank(4), 0:S2], w3s[:, k:k + 1], h2[:, k, :],
                                           start=(k == 0), stop=(k == H2 // P - 1))
                ins.then_inc(back_done, 1)

            pe.wait_ge(hi_ready, NO)
            pe.wait_ge(lo_ready, NO)
            for n in range(OH_FILLS):
                if n >= 2:
                    pe.wait_ge(front_free, n - 1)
                onehot_fill(0, n, n % 2)
            pe.wait_ge(ident_ready, 1)

            def pair(p, par, last):
                first = isinstance(p, int) and p == 0
                fills = list(enumerate(front_fills(last)))
                half = T_FILLS // 2

                def fill_until(kind, u, c):
                    while fills:
                        k, (kd, fu, fc) = fills.pop(0)
                        if kd == "T":
                            transpose_fill(p, par, k, fu, fc)
                        else:
                            front_wait(p, k)
                            onehot_fill(p + 1, fc, front_bank(par, k))
                        if (kd, fu, fc) == (kind, u, c):
                            return

                fill_until("T", 0, T_FILLS - 1)
                if not last:
                    fill_until("O", None, 1)
                if first:
                    pe.wait_ge(pads_ready, 2)
                gram_tile(p, par, 0, last)
                if not first:
                    pair_transposes(2 * p - 1, 1, back_index(p, 0), back_bank(0))
                fill_until("T", 1, half - 1)
                if not first:
                    pe.wait_ge(weights_in, 16 * 6)
                    layer1(p, 1 - par)
                fill_until("T", 1, T_FILLS - 1)
                if not first:
                    layer2(p)
                if not last:
                    fill_until("O", None, OH_FILLS - 1)
                if not first:
                    layer3(p)
                gram_tile(p, par, 1, last)
                pair_transposes(2 * p, 0, back_index(p, 5), back_bank(5), first)

            run_pairs(pe, pair)
            pair_transposes(TILES - 1, 1, back_index(PAIRS, 0), back_bank(0))
            layer1(PAIRS, (PAIRS - 1) % 2)
            layer2(PAIRS)
            layer3(PAIRS)

        @block.scalar
        def _(act):
            for o in range(NO):
                act.wait_ge(table_in[o], 16)
                nc.scalar.copy(tab_hi[0:OH_P, o, :, :].rearrange("p k d -> p (k d)"), raw_table(o)).then_inc(hi_ready, 1)

            def onehot_copy(p, n, bank, s0):
                act.wait_ge(used, RING * (OH_FILLS * p + n + 1))
                for a in range(2):
                    src = front[:, bank, a * S2:(a + 1) * S2].rearrange("p (s j g) -> p s j g", s=2, j=SPG)
                    dst = ct[:, s0:s0 + 2, :, :, NG + 1 + 2 * n + a].rearrange("p s g j -> p s j g")
                    ins = nc.scalar.copy(dst, src)
                ins.then_inc(front_free, 1)

            def transpose_copy(p, par, k, u, c):
                bank = front_bank(par, k)
                slot = 2 * par + u
                c0, c1 = c * TCH, min((c + 1) * TCH, NG + 1)
                act.wait_ge(transposed, T_FILLS * (2 * p + u) + c + 1)
                src = front[:, bank, 0:(c1 - c0) * P].rearrange("p (f j g) -> p f j g", j=SPG, g=GROUPS)
                ins = nc.scalar.copy(ct[:, slot, :, :, c0:c1].rearrange("p g j f -> p f j g"), src)
                if c1 == NG + 1:
                    ins = nc.scalar.copy(dt[:, par, u * P:(u + 1) * P], front[:, bank, (NG - c0) * P:(NG - c0 + 1) * P])
                ins.then_inc(front_free, 1)

            def gram_copy(p, u):
                t = 2 * p + u
                for c in range(GCHUNKS):
                    act.wait_ge(gram_done, GCHUNKS * t + c + 1)
                    if c == 0 and not (isinstance(p, int) and p == 0 and u == 0):
                        act.wait_ge(z1_turned, t)
                    for j in (0, 1):
                        ins = nc.scalar.copy(z1[QUAD * j:QUAD * (j + 1), c * CG:(c + 1) * CG, :],
                                             gram[QUAD * j:QUAD * (j + 1), c % 2, :, NF * j:NF * (j + 1)])
                    ins.then_inc(gram_act, 1)

            def zt_copy(index, bank, q, u):
                act.wait_ge(back_done, index + 1)
                nc.scalar.copy(zt[0:ZP, q, :, u * P:(u + 1) * P],
                               back[0:ZP, bank, 0:ZK * P].rearrange("p (k s) -> p k s", k=ZK)).then_inc(back_free, 1)

            def hidden_copy(p, k, h, m, bias):
                act.wait_ge(back_done, back_index(p, k) + 1)
                for n in range(2):
                    ins = nc.scalar.activation(h[:, m + n, :], back[:, back_bank(k), n * S2:(n + 1) * S2], ACT.Relu,
                                               bias=bias[:, m + n:m + n + 1])
                ins.then_inc(back_free, 1)

            def y_store(p):
                act.wait_ge(back_done, back_index(p, 4) + 1)
                nc.scalar.copy(yrow[0:1, 0, :], back[0:1, back_bank(4), 0:S2]).then_inc(back_free, 1)
                act.wait_ge(back_free, back_index(p, 4) + 1)
                act.dma_start(out[bass.ds((p - 1) * S2, S2), :].rearrange("s a -> a s"), yrow[0:1, 0, :]
                              ).then_inc(y_out, 16)

            for n in range(OH_FILLS):
                if n == 0:
                    act.wait_ge(pads_ready, 1)
                onehot_copy(0, n, n % 2, 0)

            def pair(p, par, last):
                first = isinstance(p, int) and p == 0
                fills = list(enumerate(front_fills(last)))
                half = T_FILLS // 2
                if first:
                    act.wait_ge(pads_ready, 2)

                def copy_until(kind, u, c):
                    while fills:
                        k, (kd, fu, fc) = fills.pop(0)
                        if kd == "T":
                            transpose_copy(p, par, k, fu, fc)
                        else:
                            onehot_copy(p + 1, fc, front_bank(par, k), 2 * (1 - par))
                        if (kd, fu, fc) == (kind, u, c):
                            return

                copy_until("T", 0, T_FILLS - 1)
                if not last:
                    copy_until("O", None, 1)
                gram_copy(p, 0)
                if not first:
                    zt_copy(back_index(p, 0), back_bank(0), 1 - par, 1)
                copy_until("T", 1, half - 1)
                if not first:
                    act.wait_ge(weights_in, 16 * 6)
                    hidden_copy(p, 1, h1, 0, b1s)
                    hidden_copy(p, 2, h1, 2, b1s)
                copy_until("T", 1, T_FILLS - 1)
                if not first:
                    hidden_copy(p, 3, h2, 0, b2s)
                if not last:
                    copy_until("O", None, OH_FILLS - 1)
                if not first:
                    y_store(p)
                gram_copy(p, 1)
                if not first:
                    act.wait_ge(y_out, 16 * p)
                zt_copy(back_index(p, 5), back_bank(5), par, 0)

            run_pairs(act, pair)
            zt_copy(back_index(PAIRS, 0), back_bank(0), (PAIRS - 1) % 2, 1)
            hidden_copy(PAIRS, 1, h1, 0, b1s)
            hidden_copy(PAIRS, 2, h1, 2, b1s)
            hidden_copy(PAIRS, 3, h2, 0, b2s)
            y_store(PAIRS)
            act.wait_ge(y_out, 16 * PAIRS)

        @block.vector
        def _(dve):
            dve.wait_ge(rowid_ready, 1)
            nc.vector.tensor_copy(rowid[:, :], rowid_i[:, :]).then_inc(const_cast, 1)
            nc.vector.memset(ct[:, 0:2, :, :, NF:QUAD], 0.0).then_inc(pads_ready, 1)
            for o in range(NO):
                dve.wait_ge(hi_ready, o + 1)
                nc.vector.tensor_sub(tab_lo[0:OH_P, o, :, :].rearrange("p k d -> p (k d)"), raw_table(o),
                                     tab_hi[0:OH_P, o, :, :].rearrange("p k d -> p (k d)")).then_inc(lo_ready, 1)
            dve.wait_ge(lo_ready, NO)
            nc.vector.memset(ct[:, 2:4, :, :, NF:QUAD], 0.0).then_inc(pads_ready, 1)
            dve.wait_ge(const_cast, 1)

            def build_onehots(p, n):
                dve.wait_ge(idb_in[n], 16 * (p + 1))
                for a in range(2):
                    for k in range(OH_K):
                        if not (isinstance(p, int) and p == 0 and n == 0):
                            dve.wait_ge(used, RING * (OH_FILLS * p + n - 1) + a * OH_K + k + 1)
                        nc.vector.tensor_scalar(ring[0:OH_P, a * OH_K + k, :], idb[0:OH_P, 2 * n + a, :],
                                                rowid[0:OH_P, k:k + 1], None, ALU.is_equal).then_inc(built, 1)

            def gram_copy(p, u):
                t = 2 * p + u
                for c in range(GCHUNKS):
                    dve.wait_ge(gram_done, GCHUNKS * t + c + 1)
                    if c == 0 and not (isinstance(p, int) and p == 0 and u == 0):
                        dve.wait_ge(z1_turned, t)
                    for j in (2, 3):
                        ins = nc.vector.tensor_copy(z1[QUAD * j:QUAD * (j + 1), c * CG:(c + 1) * CG, :],
                                                    gram[QUAD * j:QUAD * (j + 1), c % 2, :, NF * j:NF * (j + 1)])
                    ins.then_inc(gram_dve, 1)

            def pick_pairs(p, u):
                t = 2 * p + u
                first = isinstance(p, int) and p == 0
                dve.wait_ge(gram_act, GCHUNKS * (t + 1))
                dve.wait_ge(gram_dve, GCHUNKS * (t + 1))
                if not (first and u == 0):
                    dve.wait_ge(pairs_ready, t)
                nc.vector.transpose(z2[:, :, 0:QUAD], z1[:, :, :].rearrange("p g f -> p f g")).then_inc(z1_turned, 1)
                dve.wait_ge(z1_turned, t + 1)
                nc.vector.tensor_copy(z2[:, TOP:NF, NF:PITCH], z2[:, TOP:NF, 0:HALF]).then_inc(z2_wrapped, 1)
                if not first:
                    dve.wait_ge(back_done, BACK * (p - 1) + 1 + u)
                flat = z2[:, :, :].rearrange("p g f -> p (g f)")
                step = PITCH + 1

                def window(r0, n):
                    a = r0 * PITCH + r0 + 1
                    return flat_windows(flat, a, n, step, HALF)

                nc.vector.tensor_copy(zc[:, u, 0:TOP * HALF].rearrange("p (g k) -> p g k", k=HALF), window(0, TOP))
                dve.wait_ge(z2_wrapped, t + 1)
                nc.vector.tensor_copy(zc[:, u, TOP * HALF:NPAIR].rearrange("p (g k) -> p g k", k=HALF),
                                      window(TOP, HALF)).then_inc(pairs_ready, 1)

            for n in range(OH_FILLS):
                build_onehots(0, n)

            def pair(p, par, last):
                if not last:
                    build_onehots(p + 1, 0)
                    build_onehots(p + 1, 1)
                gram_copy(p, 0)
                pick_pairs(p, 0)
                if not last:
                    for n in range(2, OH_FILLS):
                        build_onehots(p + 1, n)
                gram_copy(p, 1)
                pick_pairs(p, 1)

            run_pairs(dve, pair)


def flat_windows(flat, start, n, step, width):
    rows = flat[:, start:start + (n - 1) * step + width]
    return bass.AP(tensor=rows.tensor, offset=rows.offset, ap=[list(rows.ap[0]), [step, n], [1, width]])


def kernel(**inputs):
    import concourse.bacc as bacc
    from concourse.bass_utils import run_bass_kernel_spmd as run

    nc = bacc.Bacc("TRN2", target_bir_lowering=False, num_devices=1)
    laid = {
        "dense": inputs["r_dense_x"],
        "ids": inputs["ids"],
        "ids_t": np.ascontiguousarray(np.asarray(inputs["ids"]).T[ONEHOT]),
        "w1": np.asarray(inputs["W_top1"])[top1_row_order()],
        "b1": inputs["b_top1"],
        "w2": inputs["W_top2"],
        "b2": inputs["b_top2"],
        "w3": inputs["W_top3"],
    }
    for f in range(26):
        laid[f"tbl_{f}"] = inputs[f"tbl_{f}"]
    arrays, aps = {}, {}
    for name, a in laid.items():
        a = np.ascontiguousarray(a)
        arrays["in_" + name] = a
        aps[name] = nc.dram_tensor("in_" + name, a.shape, mybir.dt.from_np(a.dtype), kind="ExternalInput").ap()
    out = nc.dram_tensor("out_y", (B, 1), F32, kind="ExternalOutput").ap()
    tables = [aps.pop(f"tbl_{f}") for f in range(26)]
    build(nc, out=out, tables=tables, **aps)
    r = run(nc, [arrays], core_ids=[0])
    return r.results[0]["out_y"]
```

```python
from contextlib import ExitStack

import numpy as np

import concourse.bass as bass
from concourse import mybir

P = 128
B = 2048
D = 128
NF = 27
DENSE = 26
QUAD = 32
SPG = P // QUAD
GROUPS = P // SPG
TILES = B // P
PAIRS = TILES // 2
S2 = 2 * P

ONEHOT = [1, 5, 8, 12, 13, 14]
GATHERED = [f for f in range(26) if f not in ONEHOT]
COLUMN_OF = GATHERED + [DENSE] + ONEHOT
NG = len(GATHERED)
NO = len(ONEHOT)
SPLIT = NO // 2 - 1
OH_ROWS = 1000
OH_K = 8
OH_P = OH_ROWS // OH_K
TCH = 4
TF = (NG + TCH - 1) // TCH
GC = 4
CG = GROUPS // GC
BK = 4

NPAIR = NF * (NF - 1) // 2
HALF = (NF - 1) // 2
TOP = NF - HALF
PITCH = NF + HALF
ZK = 3
ZP = NPAIR // ZK
H1, H2 = 512, 256
M1, M2 = H1 // P, H2 // P

F32 = mybir.dt.float32
F32R = mybir.dt.float32r
I32 = mybir.dt.int32
ALU = mybir.AluOpType
ACT = mybir.ActivationFunctionType


def pair_order():
    return [(g, (g + k) % NF) for g in range(NF) for k in range(1, HALF + 1)]


def top1_row_order():
    first = {}
    for i in range(NF):
        for j in range(i + 1, NF):
            first[(i, j)] = len(first)
    rows = []
    for a, b in pair_order():
        i, j = sorted((COLUMN_OF[a], COLUMN_OF[b]))
        rows.append(first[(i, j)])
    return rows + list(range(NPAIR, NPAIR + D))


def tile_steps(u, first, last):
    if u == 0:
        o = [[("O", 0, NO - 1)]] + [[("O", 1, m)] for m in range(0, SPLIT) if not last]
    else:
        o = [[("O", 1, m)] for m in range(SPLIT, NO - 1) if not last]
    o += [[]] * 4
    mlp = not (first and u == 0)
    z, l1, l2, l3 = ([("Z", 0)], [("L", 1)], [("L", 2)], [("L", 3)]) if mlp else ([], [], [], [])
    t = [[("T", c)] for c in range(TF)]
    g = [[("G", c)] for c in range(GC)]
    if last and u == 1:
        order = [t[0], t[1], z, t[2], l1, t[3], l2, l3] + t[4:] + g
    else:
        order = [t[0], t[1], o[0], t[2], t[3]] + t[4:] + [z, o[1], l1, o[2], l2, o[3], g[0], g[1], l3, g[2], g[3]]
    return [step for part in order for step in part]


def built_tables(u, last):
    if last:
        return []
    return list(range(0, SPLIT + 1)) if u == 0 else list(range(SPLIT + 1, NO))


def build(nc, dense_t, ids, ids_t, w1, b1, w2, b2, w3, out, tables):
    with ExitStack() as ctx:
        def sb(name, shape, dt=F32):
            return ctx.enter_context(nc.sbuf_tensor(name, shape, dt))

        def psum(name, shape):
            return ctx.enter_context(nc.psum_tensor(name, shape, F32))

        def sem(name):
            return ctx.enter_context(nc.semaphore(name))

        ct = sb("ct", [P, 4, GROUPS, SPG, QUAD])
        gat = sb("gat", [P, 2, NG, D])
        idx = sb("idx", [P, 2, 26], I32)
        idb = sb("idb", [P, NO, S2], I32)
        tab_hi = sb("tab_hi", [P, NO, OH_K, D], F32R)
        tab_lo = sb("tab_lo", [P, NO, OH_K, D], F32R)
        ring = sb("ring", [P, 2, OH_K, S2], F32R)
        rowid_i = sb("rowid_i", [P, OH_K], I32)
        rowid = sb("rowid", [P, OH_K])
        ident = sb("ident", [P, P])
        z1 = sb("z1", [P, GROUPS, NF])
        z2 = sb("z2", [P, NF, PITCH])
        zc = sb("zc", [P, NPAIR])
        zt = sb("zt", [P, ZK, P])
        dt = sb("dt", [P, 4, P])
        w1z = sb("w1z", [P, ZK, H1])
        w1d = sb("w1d", [P, H1])
        w2s = sb("w2s", [P, M1, H2])
        w3s = sb("w3s", [P, M2])
        b1s = sb("b1s", [P, M1])
        b2s = sb("b2s", [P, M2])
        h1 = sb("h1", [P, M1, P])
        h2 = sb("h2", [P, M2, P])
        yrow = sb("yrow", [1, P])

        front = psum("front", [P, 2, TCH, P])
        prod = psum("prod", [P, 512])
        gram = psum("gram", [P, 2, CG, P])
        back = psum("back", [P, 512])

        ids_in = [sem(f"ids_in{i}") for i in range(2)]
        dense_in = [sem(f"dense_in{i}") for i in range(4)]
        gathered = [[sem(f"gathered{i}_{c}") for c in range(TF)] for i in range(2)]
        idb_in = [sem(f"idb_in{m}") for m in range(NO)]
        table_in = [sem(f"table_in{m}") for m in range(NO)]
        weights_in = sem("weights_in")
        rowid_made = sem("rowid_made")
        ident_zeroed = sem("ident_zeroed")
        ident_ready = sem("ident_ready")
        rowid_ready = sem("rowid_ready")
        pads_ready = sem("pads_ready")
        hi_ready = sem("hi_ready")
        lo_ready = sem("lo_ready")
        transposed = sem("transposed")
        front_free = sem("front_free")
        built = sem("built")
        used = sem("used")
        prod_free = sem("prod_free")
        gram_done = sem("gram_done")
        gram_act = sem("gram_act")
        gram_dve = sem("gram_dve")
        z1_turned = sem("z1_turned")
        z2_wrapped = sem("z2_wrapped")
        pairs_ready = sem("pairs_ready")
        back_done = sem("back_done")
        back_free = sem("back_free")
        y_out = sem("y_out")

        def static(p, at_most):
            return isinstance(p, int) and p <= at_most

        def fill_columns(c):
            return range(c * TCH, min((c + 1) * TCH, NG))

        def front_bank(par, u, c):
            return (TF * (2 * par + u) + c) % 2

        def ring_half(par, m):
            return (NO * par + m) % 2

        def raw_table(m):
            flat = ct[:, 2:4, :, :, :].rearrange("p s g j f -> p (s g j f)")
            return flat[0:OH_P, m * OH_K * D:(m + 1) * OH_K * D]

        def run_pairs(eng, body):
            body(0, 0, False)
            with eng.Fori(0, (PAIRS - 2) // 2) as i:
                body(2 * i + 1, 1, False)
                body(2 * i + 2, 0, False)
            body(PAIRS - 1, (PAIRS - 1) % 2, True)

        block = ctx.enter_context(nc.Block())

        @block.sync
        def _(sp):
            def load_ids(t, u):
                sp.dma_start(idx[:, u, :], ids[bass.ds(t * P, P), :]).then_inc(ids_in[u], 16)

            def load_dense(t, slot):
                sp.dma_start(dt[:, slot, :], dense_t[:, bass.ds(t * P, P)]).then_inc(dense_in[slot], 16)

            def load_idb(p, m):
                src = ids_t[m:m + 1, bass.ds(p * S2, S2)].unsqueeze(0).to_broadcast([P, 1, S2])
                sp.dma_start(idb[:, m:m + 1, :], src).then_inc(idb_in[m], 16)

            load_ids(0, 0)
            for m in range(NO):
                load_idb(0, m)
                sp.dma_start(raw_table(m), tables[ONEHOT[m]].rearrange("(p k) d -> p (k d)", k=OH_K)
                             ).then_inc(table_in[m], 16)
                if m == 0:
                    load_ids(1, 1)
                    load_dense(0, 0)
                    load_dense(1, 1)
            sp.dma_start(w1z[0:ZP, :, :], w1[0:NPAIR, :].rearrange("(k p) n -> p k n", p=ZP)).then_inc(weights_in, 16)
            sp.dma_start(w1d[:, :], w1[NPAIR:NPAIR + D, :]).then_inc(weights_in, 16)
            sp.dma_start(w2s[:, :, :], w2.rearrange("(k p) n -> p k n", p=P)).then_inc(weights_in, 16)
            with nc.allow_non_contiguous_dma(reason="small vectors, one element per partition"):
                sp.dma_start(w3s[:, :], w3.rearrange("(k p) n -> p (k n)", p=P)).then_inc(weights_in, 16)
                sp.dma_start(b1s[:, :], b1.rearrange("(k p) -> p k", p=P)).then_inc(weights_in, 16)
                sp.dma_start(b2s[:, :], b2.rearrange("(k p) -> p k", p=P)).then_inc(weights_in, 16)

            def pair(p, par, last):
                for u in range(2):
                    t = 2 * p + u
                    if not static(p, 0):
                        sp.wait_ge(transposed, TF * (t - 1))
                        load_ids(t, u)
                        load_dense(t, 2 * par + u)
                    for m in built_tables(u, last):
                        sp.wait_ge(built, OH_K * (NO * p + m + 1))
                        load_idb(p + 1, m)

            run_pairs(sp, pair)

        @block.gpsimd
        def _(pool):
            nc.gpsimd.iota(rowid_i[:, :], pattern=[[1, OH_K]], base=0, channel_multiplier=OH_K).then_inc(rowid_made, 1)
            nc.gpsimd.memset(ident[:, :], 0.0).then_inc(ident_zeroed, 1)
            pool.wait_ge(ident_zeroed, 1)
            nc.gpsimd.affine_select(out=ident[:, :], in_=ident[:, :], compare_op=ALU.not_equal, fill=1.0, base=0,
                                    pattern=[[-1, P]], channel_multiplier=1).then_inc(ident_ready, 1)

            def pair(p, par, last):
                for u in range(2):
                    t = 2 * p + u
                    pool.wait_ge(ids_in[u], 16 * (p + 1))
                    pool.nop(nofuse=True)
                    for c in range(TF):
                        if not static(p, 0):
                            pool.wait_ge(transposed, TF * (t - 2) + c + 1)
                            pool.nop(nofuse=True)
                        for i in fill_columns(c):
                            f = GATHERED[i]
                            nc.gpsimd.indirect_dma_start(
                                out=gat[:, u, i, :], out_offset=None, in_=tables[f][:, :],
                                in_offset=bass.IndirectOffsetOnAxis(ap=idx[:, u, f:f + 1], axis=0),
                            ).then_inc(gathered[u][c], 16)

            run_pairs(pool, pair)

        @block.tensor
        def _(pe):
            def transpose_fill(p, par, u, c):
                t = 2 * p + u
                pe.wait_ge(gathered[u][c], 16 * len(fill_columns(c)) * (p + 1))
                if not (static(p, 0) and TF * t + c < 2):
                    pe.wait_ge(front_free, TF * t + c - 1)
                for n, col in enumerate(fill_columns(c)):
                    ins = nc.tensor.transpose(front[:, front_bank(par, u, c), n, :], gat[:, u, col, :], ident[:, :])
                ins.then_inc(transposed, 1)

            def onehot_products(p, par, m):
                n = NO * p + m
                half = ring_half(par, m)
                if not (static(p, 0) and m == 0):
                    pe.wait_ge(prod_free, n)
                for k in range(OH_K):
                    pe.wait_ge(built, OH_K * n + k + 1)
                    nc.tensor.matmul(prod[:, 0:S2], tab_hi[0:OH_P, m, k, :], ring[0:OH_P, half, k, :],
                                     start=(k == 0), stop=False)
                    nc.tensor.matmul(prod[:, 0:S2], tab_lo[0:OH_P, m, k, :], ring[0:OH_P, half, k, :],
                                     start=False, stop=(k == OH_K - 1)).then_inc(used, 1)

            def gram_chunk(p, par, u, c):
                t = 2 * p + u
                n = GC * t + c
                if c == 0:
                    pe.wait_ge(front_free, TF * (t + 1))
                if not (static(p, 0) and u == 0 and c < 2):
                    pe.wait_ge(gram_act, n - 1)
                    pe.wait_ge(gram_dve, n - 1)
                for i in range(CG):
                    four = ct[:, 2 * par + u, c * CG + i, :, :]
                    ins = nc.tensor.matmul(gram[:, c % 2, i, 0:SPG * NF].rearrange("p (j f) -> p j f", j=SPG),
                                           four.rearrange("p j f -> p (j f)"), four[:, :, 0:NF], start=True, stop=True)
                ins.then_inc(gram_done, 1)

            def transpose_pairs(t):
                pe.wait_ge(pairs_ready, t + 1)
                if not static(t, 0):
                    pe.wait_ge(back_free, BK * t)
                for k in range(ZK):
                    ins = nc.tensor.transpose(back[0:ZP, k * P:(k + 1) * P], zc[:, k * ZP:(k + 1) * ZP], ident[:, :])
                ins.then_inc(back_done, 1)

            def layer(t, n, slot):
                if n == 1 and static(t, 0):
                    pe.wait_ge(weights_in, 16 * 6)
                pe.wait_ge(back_free, BK * t + n)
                if n == 1:
                    for m in range(M1):
                        dst, units = back[:, m * P:(m + 1) * P], slice(m * P, (m + 1) * P)
                        nc.tensor.matmul(dst, w1d[:, units], dt[:, slot, :], start=True, stop=False)
                        for k in range(ZK):
                            ins = nc.tensor.matmul(dst, w1z[0:ZP, k, units], zt[0:ZP, k, :],
                                                   start=False, stop=(k == ZK - 1))
                elif n == 2:
                    for m in range(M2):
                        for k in range(M1):
                            ins = nc.tensor.matmul(back[:, m * P:(m + 1) * P], w2s[:, k, m * P:(m + 1) * P], h1[:, k, :],
                                                   start=(k == 0), stop=(k == M1 - 1))
                else:
                    for k in range(M2):
                        ins = nc.tensor.matmul(back[0:1, 0:P], w3s[:, k:k + 1], h2[:, k, :],
                                               start=(k == 0), stop=(k == M2 - 1))
                ins.then_inc(back_done, 1)

            for m in range(NO - 1):
                pe.wait_ge(hi_ready, m + 1)
                pe.wait_ge(lo_ready, m + 1)
                onehot_products(0, 0, m)
            pe.wait_ge(hi_ready, NO)
            pe.wait_ge(lo_ready, NO)
            pe.wait_ge(ident_ready, 1)
            pe.wait_ge(pads_ready, 2)

            def pair(p, par, last):
                for u in range(2):
                    t = 2 * p + u
                    for kind, *q, n in tile_steps(u, static(p, 0), last):
                        if kind == "T":
                            transpose_fill(p, par, u, n)
                        elif kind == "O":
                            onehot_products(p + q[0], (par + q[0]) % 2, n)
                        elif kind == "G":
                            gram_chunk(p, par, u, n)
                        elif kind == "Z":
                            transpose_pairs(t - 1)
                        else:
                            layer(t - 1, n, (2 * par + u - 1) % 4)

            run_pairs(pe, pair)
            transpose_pairs(TILES - 1)
            for n in (1, 2, 3):
                layer(TILES - 1, n, (TILES - 1) % 4)

        @block.scalar
        def _(act):
            def copy_products(p, par, m):
                act.wait_ge(used, OH_K * (NO * p + m + 1))
                src = prod[:, 0:S2].rearrange("p (s j g) -> p s j g", s=2, j=SPG)
                dst = ct[:, 2 * par:2 * par + 2, :, :, NG + 1 + m].rearrange("p s g j -> p s j g")
                nc.scalar.copy(dst, src).then_inc(prod_free, 1)

            def copy_fill(p, par, u, c):
                t = 2 * p + u
                slot = 2 * par + u
                act.wait_ge(transposed, TF * t + c + 1)
                if c == 2:
                    act.wait_ge(dense_in[slot], (16 * (p // 2 + 1)) if isinstance(p, int) else 8 * (p + (2 - par)))
                    nc.scalar.copy(ct[:, slot, :, :, NG].rearrange("p g j -> p j g"),
                                   dt[:, slot, :].rearrange("p (j g) -> p j g", j=SPG))
                cols = fill_columns(c)
                src = front[:, front_bank(par, u, c), 0:len(cols), :].rearrange("p f (j g) -> p f j g", j=SPG)
                nc.scalar.copy(ct[:, slot, :, :, cols.start:cols.stop].rearrange("p g j f -> p f j g"), src
                               ).then_inc(front_free, 1)

            def copy_gram(p, u, c):
                t = 2 * p + u
                act.wait_ge(gram_done, GC * t + c + 1)
                if c == 0 and not (static(p, 0) and u == 0):
                    act.wait_ge(z1_turned, t)
                for j in (0, 1):
                    ins = nc.scalar.copy(z1[QUAD * j:QUAD * (j + 1), c * CG:(c + 1) * CG, :],
                                         gram[QUAD * j:QUAD * (j + 1), c % 2, :, NF * j:NF * (j + 1)])
                ins.then_inc(gram_act, 1)

            def copy_pairs(t):
                act.wait_ge(back_done, BK * t + 1)
                nc.scalar.copy(zt[0:ZP, :, :].rearrange("p k s -> p (k s)"), back[0:ZP, 0:ZK * P]).then_inc(back_free, 1)

            def finish_layer(t, n):
                act.wait_ge(back_done, BK * t + n + 1)
                if n < 3:
                    h, bias, blocks = ((h1, b1s, M1), (h2, b2s, M2))[n - 1]
                    for m in range(blocks):
                        ins = nc.scalar.activation(h[:, m, :], back[:, m * P:(m + 1) * P], ACT.Relu, bias=bias[:, m:m + 1])
                    ins.then_inc(back_free, 1)
                else:
                    if not static(t, 0):
                        act.wait_ge(y_out, 16 * t)
                    nc.scalar.copy(yrow[0:1, :], back[0:1, 0:P]).then_inc(back_free, 1)
                    act.wait_ge(back_free, BK * (t + 1))
                    act.dma_start(out[bass.ds(t * P, P), :].rearrange("s a -> a s"), yrow[0:1, :]).then_inc(y_out, 16)

            for m in range(NO):
                act.wait_ge(table_in[m], 16)
                nc.scalar.copy(tab_hi[0:OH_P, m, :, :].rearrange("p k d -> p (k d)"), raw_table(m)).then_inc(hi_ready, 1)
                if m == 2:
                    act.wait_ge(pads_ready, 1)
                if m >= 2:
                    copy_products(0, 0, m - 2)
            for m in range(NO - 2, NO - 1):
                copy_products(0, 0, m)
            act.wait_ge(pads_ready, 2)
            act.wait_ge(weights_in, 16 * 6)

            def pair(p, par, last):
                for u in range(2):
                    t = 2 * p + u
                    for kind, *q, n in tile_steps(u, static(p, 0), last):
                        if kind == "T":
                            copy_fill(p, par, u, n)
                        elif kind == "O":
                            copy_products(p + q[0], (par + q[0]) % 2, n)
                        elif kind == "G":
                            copy_gram(p, u, n)
                        elif kind == "Z":
                            copy_pairs(t - 1)
                        else:
                            finish_layer(t - 1, n)

            run_pairs(act, pair)
            copy_pairs(TILES - 1)
            for n in (1, 2, 3):
                finish_layer(TILES - 1, n)
            act.wait_ge(y_out, 16 * TILES)

        @block.vector
        def _(dve):
            dve.wait_ge(rowid_made, 1)
            nc.vector.tensor_copy(rowid[:, :], rowid_i[:, :]).then_inc(rowid_ready, 1)
            nc.vector.memset(ct[:, 0:2, :, :, NF:QUAD], 0.0).then_inc(pads_ready, 1)
            dve.wait_ge(rowid_ready, 1)

            def build_onehots(p, par, m):
                n = NO * p + m
                dve.wait_ge(idb_in[m], 16 * (p + 1))
                for k in range(OH_K):
                    if not (static(p, 0) and m < 2):
                        dve.wait_ge(used, OH_K * (n - 2) + k + 1)
                    nc.vector.tensor_scalar(ring[0:OH_P, ring_half(par, m), k, :], idb[0:OH_P, m, :],
                                            rowid[0:OH_P, k:k + 1], None, ALU.is_equal).then_inc(built, 1)

            def copy_gram(p, u, c):
                t = 2 * p + u
                dve.wait_ge(gram_done, GC * t + c + 1)
                if c == 0 and not (static(p, 0) and u == 0):
                    dve.wait_ge(z1_turned, t)
                for j in (2, 3):
                    ins = nc.vector.tensor_copy(z1[QUAD * j:QUAD * (j + 1), c * CG:(c + 1) * CG, :],
                                                gram[QUAD * j:QUAD * (j + 1), c % 2, :, NF * j:NF * (j + 1)])
                ins.then_inc(gram_dve, 1)

            def pick_pairs(t):
                dve.wait_ge(gram_act, GC * (t + 1))
                dve.wait_ge(gram_dve, GC * (t + 1))
                if not static(t, 0):
                    dve.wait_ge(pairs_ready, t)
                nc.vector.transpose(z2[:, :, 0:QUAD], z1[:, :, :].rearrange("p g f -> p f g")).then_inc(z1_turned, 1)
                dve.wait_ge(z1_turned, t + 1)
                nc.vector.tensor_copy(z2[:, TOP:NF, NF:PITCH], z2[:, TOP:NF, 0:HALF]).then_inc(z2_wrapped, 1)
                if not static(t, 0):
                    dve.wait_ge(back_done, BK * (t - 1) + 1)
                nc.vector.tensor_copy(zc[:, 0:TOP * HALF].rearrange("p (g k) -> p g k", k=HALF), windows(z2, 0, TOP))
                dve.wait_ge(z2_wrapped, t + 1)
                nc.vector.tensor_copy(zc[:, TOP * HALF:NPAIR].rearrange("p (g k) -> p g k", k=HALF),
                                      windows(z2, TOP, HALF)).then_inc(pairs_ready, 1)

            for m in range(NO):
                dve.wait_ge(hi_ready, m + 1)
                nc.vector.tensor_sub(tab_lo[0:OH_P, m, :, :].rearrange("p k d -> p (k d)"), raw_table(m),
                                     tab_hi[0:OH_P, m, :, :].rearrange("p k d -> p (k d)")).then_inc(lo_ready, 1)
                build_onehots(0, 0, m)
            dve.wait_ge(lo_ready, NO)
            nc.vector.memset(ct[:, 2:4, :, :, NF:QUAD], 0.0).then_inc(pads_ready, 1)

            def pair(p, par, last):
                for u in range(2):
                    if not (static(p, 0) and u == 0):
                        pick_pairs(2 * p + u - 1)
                    for m in built_tables(u, last):
                        build_onehots(p + 1, 1 - par, m)
                    for c in range(GC):
                        copy_gram(p, u, c)

            run_pairs(dve, pair)
            pick_pairs(TILES - 1)


def windows(z2, row, n):
    flat = z2[:, :, :].rearrange("p g f -> p (g f)")
    start = row * PITCH + row + 1
    rows = flat[:, start:start + (n - 1) * (PITCH + 1) + HALF]
    return bass.AP(tensor=rows.tensor, offset=rows.offset, ap=[list(rows.ap[0]), [PITCH + 1, n], [1, HALF]])


def kernel(**inputs):
    import concourse.bacc as bacc
    from concourse.bass_utils import run_bass_kernel_spmd as run

    nc = bacc.Bacc("TRN2", target_bir_lowering=False, num_devices=1)
    laid = {
        "dense_t": np.asarray(inputs["r_dense_x"]).T,
        "ids": inputs["ids"],
        "ids_t": np.ascontiguousarray(np.asarray(inputs["ids"]).T[ONEHOT]),
        "w1": np.asarray(inputs["W_top1"])[top1_row_order()],
        "b1": inputs["b_top1"],
        "w2": inputs["W_top2"],
        "b2": inputs["b_top2"],
        "w3": inputs["W_top3"],
    }
    for f in range(26):
        laid[f"tbl_{f}"] = inputs[f"tbl_{f}"]
    arrays, aps = {}, {}
    for name, a in laid.items():
        a = np.ascontiguousarray(a)
        arrays["in_" + name] = a
        aps[name] = nc.dram_tensor("in_" + name, a.shape, mybir.dt.from_np(a.dtype), kind="ExternalInput").ap()
    out = nc.dram_tensor("out_y", (B, 1), F32, kind="ExternalOutput").ap()
    tables = [aps.pop(f"tbl_{f}") for f in range(26)]
    build(nc, out=out, tables=tables, **aps)
    r = run(nc, [arrays], core_ids=[0])
    return r.results[0]["out_y"]
```

```python
from contextlib import ExitStack

import numpy as np

import concourse.bass as bass
from concourse import mybir

P = 128
B = 2048
D = 128
NF = 27
DENSE = 26
QUAD = 32
SPG = P // QUAD
GROUPS = P // SPG
TILES = B // P
PAIRS = TILES // 2
S2 = 2 * P

ONEHOT = [1, 5, 8, 12, 13, 14]
EXTRA = [21, 24, 25]
GATHERED = [f for f in range(26) if f not in ONEHOT + EXTRA] + EXTRA
COLUMN_OF = GATHERED + [DENSE] + ONEHOT
NG = len(GATHERED)
NO = len(ONEHOT)
NX = len(EXTRA)
NT = NO + min(NX, 2)
SPLIT = NO // 2 - 1
OH_ROWS = 1000
OH_K = 8
OH_P = OH_ROWS // OH_K
TCH = 4
TF = (NG + TCH - 1) // TCH
GC = 4
CG = GROUPS // GC
BK = 4

NPAIR = NF * (NF - 1) // 2
HALF = (NF - 1) // 2
TOP = NF - HALF
PITCH = NF + HALF
ZK = 3
ZP = NPAIR // ZK
H1, H2 = 512, 256
M1, M2 = H1 // P, H2 // P

F32 = mybir.dt.float32
F32R = mybir.dt.float32r
I32 = mybir.dt.int32
ALU = mybir.AluOpType
ACT = mybir.ActivationFunctionType


def pair_order():
    return [(g, (g + k) % NF) for g in range(NF) for k in range(1, HALF + 1)]


def top1_row_order():
    first = {}
    for i in range(NF):
        for j in range(i + 1, NF):
            first[(i, j)] = len(first)
    rows = []
    for a, b in pair_order():
        i, j = sorted((COLUMN_OF[a], COLUMN_OF[b]))
        rows.append(first[(i, j)])
    return rows + list(range(NPAIR, NPAIR + D))


def tile_steps(u, first, last):
    t = [[("T", c)] for c in range(TF)]
    g = [[("G", c)] for c in range(GC)]
    z, l1, l2, l3 = [("Z", 0)], [("L", 1)], [("L", 2)], [("L", 3)]
    if first and u == 0:
        o = [[("O", 0, m)] for m in range(NO + NX)]
        order = o[:2] + [t[0], o[2], t[1], o[3], t[2], o[4], t[3], o[5], t[4]] + g[:2] + [o[6]] + g[2:] + o[7:]
    elif first:
        o = [[("O", 1, m)] for m in range(NO - 1)]
        order = [t[0], t[1], o[0], t[2], t[3], o[1], z, t[4]]
        order += o[2:4] + [l1] + o[4:] + [l2, g[0], g[1], l3, g[2], g[3]]
    elif last and u == 0:
        order = t[:2] + [[("O", 0, NO - 1)]] + t[2:] + [z, g[0], l1, g[1], g[2], g[3]]
    elif last:
        order = t[:2] + [[("M", 2)]] + t[2:] + [[("M", 3)], g[0], z] + g[1:]
    else:
        if u == 0:
            o = [[("O", 0, NO - 1)]] + [[("O", 1, m)] for m in range(0, SPLIT)]
        else:
            o = [[("O", 1, m)] for m in range(SPLIT, NO - 1)]
        order = [t[0], t[1], o[0]] + t[2:-1] + [z, t[-1], o[1], l1, o[2], l2, g[0], g[1], l3, g[2], g[3]]
    return [step for part in order for step in part]


X, Y = TILES - 2, TILES - 1
TAIL = ([("L", X, 1, m, 0) for m in range(4)] + [("Z", Y, 0, 0, 0)] + [("L", X, 2, m, 0) for m in range(2)]
        + [("L", Y, 1, m, 4) for m in range(4)] + [("L", X, 3, 0, 5)] + [("L", Y, 2, m, 7) for m in range(2)]
        + [("L", Y, 3, 0, 12)])


def built_tables(u):
    return list(range(0, SPLIT + 1)) if u == 0 else list(range(SPLIT + 1, NO))


def build(nc, dense_t, ids, ids_t, w1, b1, w2, b2, w3, out, tables):
    with ExitStack() as ctx:
        def sb(name, shape, dt=F32):
            return ctx.enter_context(nc.sbuf_tensor(name, shape, dt))

        def psum(name, shape):
            return ctx.enter_context(nc.psum_tensor(name, shape, F32))

        def sem(name):
            return ctx.enter_context(nc.semaphore(name))

        ct = sb("ct", [P, 4, GROUPS, SPG, QUAD])
        gat = sb("gat", [P, 2, NG, D])
        idx = sb("idx", [P, 2, 26], I32)
        idb = sb("idb", [P, NO + NX, S2], I32)
        tab_hi = sb("tab_hi", [P, NT, OH_K, D], F32R)
        tab_lo = sb("tab_lo", [P, NT, OH_K, D], F32R)
        ring = sb("ring", [P, 2, OH_K, S2], F32R)
        rowid_i = sb("rowid_i", [P, OH_K], I32)
        rowid = sb("rowid", [P, OH_K])
        ident = sb("ident", [P, P])
        late = sb("late", [P, NX, S2])
        z1 = sb("z1", [P, GROUPS, NF])
        z2 = sb("z2", [P, NF, PITCH])
        zc = sb("zc", [P, NPAIR])
        zt = sb("zt", [P, ZK, P])
        dt = sb("dt", [P, 4, P])
        w1z = sb("w1z", [P, ZK, H1])
        w1d = sb("w1d", [P, H1])
        w2s = sb("w2s", [P, M1, H2])
        w3s = sb("w3s", [P, M2])
        b1s = sb("b1s", [P, M1])
        b2s = sb("b2s", [P, M2])
        h1 = sb("h1", [P, M1, P])
        h2 = sb("h2", [P, M2, P])
        yrow = sb("yrow", [1, 2, P])

        front = psum("front", [P, 2, TCH, P])
        prod = psum("prod", [P, 512])
        gram = psum("gram", [P, 2, CG, P])
        back = psum("back", [P, 512])
        tail_banks = [back[:, 0:512]] + [front[:, i, :, :].rearrange("p f s -> p (f s)") for i in range(2)]
        tail_banks += [gram[:, i, 4 * k:4 * k + 4, :].rearrange("p g s -> p (g s)") for i in range(2) for k in range(2)]

        ids_in = [sem(f"ids_in{i}") for i in range(2)]
        dense_in = [sem(f"dense_in{i}") for i in range(4)]
        gathered = [[sem(f"gathered{i}_{c}") for c in range(TF)] for i in range(2)]
        idb_in = [sem(f"idb_in{m}") for m in range(NO + NX)]
        table_in = [sem(f"table_in{m}") for m in range(NO + NX)]
        weights_in = sem("weights_in")
        rowid_made = sem("rowid_made")
        ident_zeroed = sem("ident_zeroed")
        ident_ready = sem("ident_ready")
        rowid_ready = sem("rowid_ready")
        pads_ready = sem("pads_ready")
        spare_in = sem("spare_in")
        hi_ready = sem("hi_ready")
        lo_ready = sem("lo_ready")
        transposed = sem("transposed")
        front_free = sem("front_free")
        built = sem("built")
        used = sem("used")
        prod_free = sem("prod_free")
        late_placed = sem("late_placed")
        gram_done = sem("gram_done")
        gram_act = sem("gram_act")
        gram_dve = sem("gram_dve")
        z1_turned = sem("z1_turned")
        z2_wrapped = sem("z2_wrapped")
        pairs_ready = sem("pairs_ready")
        back_done = sem("back_done")
        back_free = sem("back_free")
        tail_done = sem("tail_done")
        tail_free = sem("tail_free")
        y_out = sem("y_out")
        y_last = sem("y_last")

        def static(p, at_most):
            return isinstance(p, int) and p <= at_most

        def fill_columns(c, last=False):
            return range(c * TCH, min((c + 1) * TCH, NG - NX * last))

        def order_of(p, m):
            return m if static(p, 0) else NO * p + NX + m

        def front_bank(par, u, c):
            return (TF * (2 * par + u) + c) % 2

        def ring_half(p, par, m):
            return m % 2 if static(p, 0) else (NO * par + NX + m) % 2

        def product_bank(p, m):
            return back if static(p, 0) and m % 2 else prod

        def table_slot(m):
            return m if m < NT else NO + (m - NO) % 2

        def raw_table(m):
            if m >= 8:
                return z2[:, :, :].rearrange("p g f -> p (g f)")[0:OH_P, 0:OH_K * D]
            flat = ct[:, 2:4, :, :, :].rearrange("p s g j f -> p (s g j f)")
            return flat[0:OH_P, m * OH_K * D:(m + 1) * OH_K * D]

        def run_pairs(eng, body):
            body(0, 0, False)
            with eng.Fori(0, (PAIRS - 2) // 2) as i:
                body(2 * i + 1, 1, False)
                body(2 * i + 2, 0, False)
            body(PAIRS - 1, (PAIRS - 1) % 2, True)

        block = ctx.enter_context(nc.Block())

        @block.sync
        def _(sp):
            def load_ids(t, u):
                sp.dma_start(idx[:, u, :], ids[bass.ds(t * P, P), :]).then_inc(ids_in[u], 16)

            def load_dense(t, slot):
                sp.dma_start(dt[:, slot, :], dense_t[:, bass.ds(t * P, P)]).then_inc(dense_in[slot], 16)

            def load_idb(p, m):
                src = ids_t[m:m + 1, bass.ds(p * S2, S2)].unsqueeze(0).to_broadcast([P, 1, S2])
                sp.dma_start(idb[:, m:m + 1, :], src).then_inc(idb_in[m], 16)

            load_ids(0, 0)
            for m in range(NO + NX):
                if 3 <= m < NT:
                    sp.wait_ge(hi_ready, m - 2)
                elif m == NT:
                    sp.wait_ge(transposed, TF)
                sp.dma_start(raw_table(m), tables[(ONEHOT + EXTRA)[m]].rearrange("(p k) d -> p (k d)", k=OH_K)
                             ).then_inc(table_in[m], 16)
                load_idb(0 if m < NO else PAIRS - 1, m)
                if m == 0:
                    load_ids(1, 1)
                    load_dense(0, 0)
                    load_dense(1, 1)
            sp.dma_start(ct[OH_P:P, 2:4, :, :, :].rearrange("p s g j f -> p (s g j f)"),
                         tables[0][0:(P - OH_P) * 2 * QUAD, :].rearrange("(p r) d -> p (r d)", p=P - OH_P)
                         ).then_inc(spare_in, 16)
            sp.dma_start(w1z[0:ZP, :, :], w1[0:NPAIR, :].rearrange("(k p) n -> p k n", p=ZP)).then_inc(weights_in, 16)
            sp.dma_start(w1d[:, :], w1[NPAIR:NPAIR + D, :]).then_inc(weights_in, 16)
            sp.dma_start(w2s[:, :, :], w2.rearrange("(k p) n -> p k n", p=P)).then_inc(weights_in, 16)
            with nc.allow_non_contiguous_dma(reason="small vectors, one element per partition"):
                sp.dma_start(w3s[:, :], w3.rearrange("(k p) n -> p (k n)", p=P)).then_inc(weights_in, 16)
                sp.dma_start(b1s[:, :], b1.rearrange("(k p) -> p k", p=P)).then_inc(weights_in, 16)
                sp.dma_start(b2s[:, :], b2.rearrange("(k p) -> p k", p=P)).then_inc(weights_in, 16)

            def pair(p, par, last):
                for u in range(2):
                    t = 2 * p + u
                    if not static(p, 0):
                        sp.wait_ge(transposed, TF * (t - 1))
                        load_ids(t, u)
                        load_dense(t, 2 * par + u)
                    for m in () if last else built_tables(u):
                        sp.wait_ge(built, OH_K * (order_of(p, m) + 1))
                        load_idb(p + 1, m)

            run_pairs(sp, pair)

        @block.gpsimd
        def _(pool):
            nc.gpsimd.iota(rowid_i[:, :], pattern=[[1, OH_K]], base=0, channel_multiplier=OH_K).then_inc(rowid_made, 1)
            nc.gpsimd.memset(ident[:, :], 0.0).then_inc(ident_zeroed, 1)
            pool.wait_ge(ident_zeroed, 1)
            nc.gpsimd.affine_select(out=ident[:, :], in_=ident[:, :], compare_op=ALU.not_equal, fill=1.0, base=0,
                                    pattern=[[-1, P]], channel_multiplier=1).then_inc(ident_ready, 1)
            nc.gpsimd.memset(ct[:, 0:2, :, :, NF:QUAD], 0.0).then_inc(pads_ready, 1)

            def pair(p, par, last):
                for u in range(2):
                    t = 2 * p + u
                    pool.wait_ge(ids_in[u], 16 * (p + 1))
                    pool.nop(nofuse=True)
                    for c in range(TF):
                        if not static(p, 0):
                            pool.wait_ge(transposed, TF * (t - 2) + c + 1)
                            pool.nop(nofuse=True)
                        for i in fill_columns(c, last):
                            f = GATHERED[i]
                            nc.gpsimd.indirect_dma_start(
                                out=gat[:, u, i, :], out_offset=None, in_=tables[f][:, :],
                                in_offset=bass.IndirectOffsetOnAxis(ap=idx[:, u, f:f + 1], axis=0),
                            ).then_inc(gathered[u][c], 16)

            run_pairs(pool, pair)

        @block.tensor
        def _(pe):
            def transpose_fill(p, par, u, c, last):
                t = 2 * p + u
                cols = fill_columns(c, last)
                pe.wait_ge(gathered[u][c], 16 * len(fill_columns(c)) * p + 16 * len(cols))
                if not (static(p, 0) and TF * t + c < 2):
                    pe.wait_ge(front_free, TF * t + c - 1)
                for n, col in enumerate(cols):
                    ins = nc.tensor.transpose(front[:, front_bank(par, u, c), n, :], gat[:, u, col, :], ident[:, :])
                ins.then_inc(transposed, 1)

            def onehot_products(p, par, m):
                n = order_of(p, m)
                half = ring_half(p, par, m)
                table = table_slot(m)
                if static(p, 0):
                    pe.wait_ge(hi_ready, n + 1)
                    pe.wait_ge(lo_ready, n + 1)
                bank = product_bank(p, m)
                if not static(p, 0):
                    pe.wait_ge(prod_free, n)
                elif m >= 2:
                    pe.wait_ge(prod_free, n - 1)
                for k in range(OH_K):
                    pe.wait_ge(built, OH_K * n + k + 1)
                    nc.tensor.matmul(bank[:, 0:S2], tab_hi[0:OH_P, table, k, :], ring[0:OH_P, half, k, :],
                                     start=(k == 0), stop=False)
                    nc.tensor.matmul(bank[:, 0:S2], tab_lo[0:OH_P, table, k, :], ring[0:OH_P, half, k, :],
                                     start=False, stop=(k == OH_K - 1)).then_inc(used, 1)

            def gram_chunk(p, par, u, c, last):
                t = 2 * p + u
                n = GC * t + c
                if c == 0:
                    pe.wait_ge(front_free, TF * (t + 1))
                    if static(p, 0):
                        pe.wait_ge(pads_ready, 1)
                    if last:
                        pe.wait_ge(late_placed, u + 1)
                if not (static(p, 0) and u == 0 and c < 2):
                    pe.wait_ge(gram_act, n - 1)
                    pe.wait_ge(gram_dve, n - 1)
                for i in range(CG):
                    four = ct[:, 2 * par + u, c * CG + i, :, :]
                    ins = nc.tensor.matmul(gram[:, c % 2, i, 0:SPG * NF].rearrange("p (j f) -> p j f", j=SPG),
                                           four.rearrange("p j f -> p (j f)"), four[:, :, 0:NF], start=True, stop=True)
                ins.then_inc(gram_done, 1)

            def transpose_pairs(bank):
                for k in range(ZK):
                    ins = nc.tensor.transpose(bank[0:ZP, k * P:(k + 1) * P], zc[:, k * ZP:(k + 1) * ZP], ident[:, :])
                return ins

            def layer_block(dst, n, m, slot, source=None):
                def input_ready(k):
                    if source is not None:
                        pe.wait_ge(tail_free, source + k + 1)

                units = slice(m * P, (m + 1) * P)
                if n == 1:
                    nc.tensor.matmul(dst, w1d[:, units], dt[:, slot, :], start=True, stop=False)
                    for k in range(ZK):
                        ins = nc.tensor.matmul(dst, w1z[0:ZP, k, units], zt[0:ZP, k, :], start=False, stop=(k == ZK - 1))
                elif n == 2:
                    for k in range(M1):
                        input_ready(k)
                        ins = nc.tensor.matmul(dst, w2s[:, k, units], h1[:, k, :], start=(k == 0), stop=(k == M1 - 1))
                else:
                    for k in range(M2):
                        input_ready(k)
                        ins = nc.tensor.matmul(dst[0:1, :], w3s[:, k:k + 1], h2[:, k, :], start=(k == 0), stop=(k == M2 - 1))
                return ins

            def layer(n, slot):
                for m in range((M1, M2, 1)[n - 1]):
                    ins = layer_block(back[:, m * P:(m + 1) * P], n, m, slot)
                return ins

            pe.wait_ge(ident_ready, 1)

            def pair(p, par, last):
                for u in range(2):
                    t = 2 * p + u
                    for kind, *q, n in tile_steps(u, static(p, 0), last):
                        if kind == "T":
                            transpose_fill(p, par, u, n, last)
                        elif kind == "O":
                            onehot_products(p + q[0], (par + q[0]) % 2, n)
                        elif kind == "G":
                            gram_chunk(p, par, u, n, last)
                        elif kind == "Z":
                            pe.wait_ge(pairs_ready, t)
                            if not static(t, 1):
                                pe.wait_ge(back_free, BK * (t - 1))
                            transpose_pairs(back).then_inc(back_done, 1)
                        else:
                            ago = 1 if kind == "L" else 2
                            if static(t, 1):
                                pe.wait_ge(weights_in, 16 * 6)
                            pe.wait_ge(back_free, BK * (t - ago) + n)
                            layer(n, (2 * par + u - ago) % 4).then_inc(back_done, 1)

            run_pairs(pe, pair)
            for i, (kind, t, n, m, source) in enumerate(TAIL):
                if i == 0:
                    pe.wait_ge(back_free, BK * t + 1)
                if i == 3:
                    pe.wait_ge(gram_act, GC * TILES)
                    pe.wait_ge(gram_dve, GC * TILES)
                if i > 6:
                    pe.wait_ge(tail_free, i - 6)
                if kind == "Z":
                    pe.wait_ge(pairs_ready, t + 1)
                    transpose_pairs(tail_banks[i % 7]).then_inc(tail_done, 1)
                else:
                    if (t, n) == (Y, 1):
                        pe.wait_ge(tail_free, source + 1)
                    layer_block(tail_banks[i % 7][:, 0:P], n, m, t % 4, source).then_inc(tail_done, 1)

        @block.scalar
        def _(act):
            def copy_products(p, par, m):
                act.wait_ge(used, OH_K * (order_of(p, m) + 1))
                if m >= NO:
                    nc.scalar.copy(late[:, m - NO, :], product_bank(p, m)[:, 0:S2]).then_inc(prod_free, 1)
                    return
                if static(p, 1) and p == 1:
                    act.wait_ge(lo_ready, NT)
                    act.wait_ge(spare_in, 16)
                src = product_bank(p, m)[:, 0:S2].rearrange("p (s j g) -> p s j g", s=2, j=SPG)
                dst = ct[:, 2 * par:2 * par + 2, :, :, NG + 1 + m].rearrange("p s g j -> p s j g")
                nc.scalar.copy(dst, src).then_inc(prod_free, 1)

            def place_late(par, u):
                src = late[:, :, u * P:(u + 1) * P].rearrange("p e (j g) -> p e j g", j=SPG)
                nc.scalar.copy(ct[:, 2 * par + u, :, :, NG - NX:NG].rearrange("p g j e -> p e j g"), src
                               ).then_inc(late_placed, 1)

            def copy_fill(p, par, u, c, last):
                t = 2 * p + u
                slot = 2 * par + u
                if c == TF - 1:
                    act.wait_ge(dense_in[slot], (16 * (p // 2 + 1)) if isinstance(p, int) else 8 * (p + (2 - par)))
                    nc.scalar.copy(ct[:, slot, :, :, NG].rearrange("p g j -> p j g"),
                                   dt[:, slot, :].rearrange("p (j g) -> p j g", j=SPG))
                act.wait_ge(transposed, TF * t + c + 1)
                cols = fill_columns(c, last)
                src = front[:, front_bank(par, u, c), 0:len(cols), :].rearrange("p f (j g) -> p f j g", j=SPG)
                nc.scalar.copy(ct[:, slot, :, :, cols.start:cols.stop].rearrange("p g j f -> p f j g"), src
                               ).then_inc(front_free, 1)

            def copy_gram(p, u, c):
                t = 2 * p + u
                act.wait_ge(gram_done, GC * t + c + 1)
                if c == 0 and not (static(p, 0) and u == 0):
                    act.wait_ge(z1_turned, t)
                for j in (0, 1):
                    ins = nc.scalar.copy(z1[QUAD * j:QUAD * (j + 1), c * CG:(c + 1) * CG, :],
                                         gram[QUAD * j:QUAD * (j + 1), c % 2, :, NF * j:NF * (j + 1)])
                ins.then_inc(gram_act, 1)

            def copy_pairs(bank, free):
                nc.scalar.copy(zt[0:ZP, :, :].rearrange("p k s -> p (k s)"), bank[0:ZP, 0:ZK * P]).then_inc(free, 1)

            def finish_block(src, n, m):
                h, bias = ((h1, b1s), (h2, b2s))[n - 1]
                return nc.scalar.activation(h[:, m, :], src, ACT.Relu, bias=bias[:, m:m + 1])

            def store_result(bank, t, row, free, count, stored):
                nc.scalar.copy(yrow[0:1, row, :], bank[0:1, 0:P]).then_inc(free, 1)
                act.wait_ge(free, count)
                act.dma_start(out[bass.ds(t * P, P), :].rearrange("s a -> a s"), yrow[0:1, row, :]).then_inc(stored, 16)

            def split_high(m):
                act.wait_ge(table_in[m], 16)
                if m >= NT:
                    act.wait_ge(used, OH_K * (m - 1))
                nc.scalar.copy(tab_hi[0:OH_P, table_slot(m), :, :].rearrange("p k d -> p (k d)"), raw_table(m)
                               ).then_inc(hi_ready, 1)

            split_high(0)
            split_high(1)

            def pair(p, par, last):
                for u in range(2):
                    t = 2 * p + u
                    for kind, *q, n in tile_steps(u, static(p, 0), last):
                        if last and (kind, n) == ("T", 0):
                            act.wait_ge(gram_done, GC * (t - 3))
                            place_late(par, u)
                        if kind == "T":
                            copy_fill(p, par, u, n, last)
                        elif kind == "O":
                            if static(p, 0) and q == [0] and n + 2 < NT:
                                split_high(n + 2)
                            copy_products(p + q[0], (par + q[0]) % 2, n)
                            if static(p, 0) and q == [0] and NT <= n + 2 < NO + NX:
                                split_high(n + 2)
                        elif kind == "G":
                            copy_gram(p, u, n)
                        elif kind == "Z":
                            if static(t, 1):
                                act.wait_ge(weights_in, 16 * 6)
                            act.wait_ge(back_done, BK * (t - 1) + 1)
                            copy_pairs(back, back_free)
                        else:
                            ago = 1 if kind == "L" else 2
                            act.wait_ge(back_done, BK * (t - ago) + n + 1)
                            if n < 3:
                                for m in range((M1, M2)[n - 1]):
                                    ins = finish_block(back[:, m * P:(m + 1) * P], n, m)
                                ins.then_inc(back_free, 1)
                            else:
                                if not static(t, 1):
                                    act.wait_ge(y_out, 16 * (t - ago))
                                store_result(back, t - ago, 0, back_free, BK * (t - ago + 1), y_out)

            run_pairs(act, pair)
            act.wait_ge(y_out, 16 * (TILES - 2))
            for i, (kind, t, n, m, _) in enumerate(TAIL):
                act.wait_ge(tail_done, i + 1)
                if kind == "Z":
                    copy_pairs(tail_banks[i % 7], tail_free)
                elif n < 3:
                    finish_block(tail_banks[i % 7][:, 0:P], n, m).then_inc(tail_free, 1)
                elif t == TILES - 2:
                    store_result(tail_banks[i % 7], t, 0, tail_free, i + 1, y_out)
                else:
                    store_result(tail_banks[i % 7], t, 1, tail_free, i + 1, y_last)
            act.wait_ge(y_out, 16 * (TILES - 1))
            act.wait_ge(y_last, 16)

        @block.vector
        def _(dve):
            dve.wait_ge(rowid_made, 1)
            nc.vector.tensor_copy(rowid[:, :], rowid_i[:, :]).then_inc(rowid_ready, 1)
            dve.wait_ge(rowid_ready, 1)

            def build_onehots(p, par, m):
                n = order_of(p, m)
                dve.wait_ge(idb_in[m], 16 * (p + 1) if m < NO else 16)
                for k in range(OH_K):
                    if not (static(p, 0) and m < 2):
                        dve.wait_ge(used, OH_K * (n - 2) + k + 1)
                    nc.vector.tensor_scalar(ring[0:OH_P, ring_half(p, par, m), k, :], idb[0:OH_P, m, :],
                                            rowid[0:OH_P, k:k + 1], None, ALU.is_equal).then_inc(built, 1)

            def copy_gram(p, u, c):
                t = 2 * p + u
                dve.wait_ge(gram_done, GC * t + c + 1)
                if c == 0 and not (static(p, 0) and u == 0):
                    dve.wait_ge(z1_turned, t)
                for j in (2, 3):
                    ins = nc.vector.tensor_copy(z1[QUAD * j:QUAD * (j + 1), c * CG:(c + 1) * CG, :],
                                                gram[QUAD * j:QUAD * (j + 1), c % 2, :, NF * j:NF * (j + 1)])
                ins.then_inc(gram_dve, 1)

            def pick_pairs(t):
                dve.wait_ge(gram_act, GC * (t + 1))
                dve.wait_ge(gram_dve, GC * (t + 1))
                if not static(t, 0):
                    dve.wait_ge(pairs_ready, t)
                nc.vector.transpose(z2[:, :, 0:QUAD], z1[:, :, :].rearrange("p g f -> p f g")).then_inc(z1_turned, 1)
                dve.wait_ge(z1_turned, t + 1)
                nc.vector.tensor_copy(z2[:, TOP:NF, NF:PITCH], z2[:, TOP:NF, 0:HALF]).then_inc(z2_wrapped, 1)
                if not static(t, 0):
                    dve.wait_ge(back_done, BK * (t - 1) + 1)
                nc.vector.tensor_copy(zc[:, 0:TOP * HALF].rearrange("p (g k) -> p g k", k=HALF), windows(z2, 0, TOP))
                dve.wait_ge(z2_wrapped, t + 1)
                nc.vector.tensor_copy(zc[:, TOP * HALF:NPAIR].rearrange("p (g k) -> p g k", k=HALF),
                                      windows(z2, TOP, HALF)).then_inc(pairs_ready, 1)

            def split_low(m):
                dve.wait_ge(hi_ready, m + 1)
                if m >= NT:
                    dve.wait_ge(used, OH_K * (m - 1))
                nc.vector.tensor_sub(tab_lo[0:OH_P, table_slot(m), :, :].rearrange("p k d -> p (k d)"), raw_table(m),
                                     tab_hi[0:OH_P, table_slot(m), :, :].rearrange("p k d -> p (k d)")
                                     ).then_inc(lo_ready, 1)

            for m in range(NO):
                split_low(m)
                build_onehots(0, 0, m)
            split_low(NO)
            build_onehots(0, 0, NO)

            def pair(p, par, last):
                for u in range(2):
                    if not (static(p, 0) and u == 0):
                        pick_pairs(2 * p + u - 1)
                    if static(p, 0) and u == 1:
                        for m in range(NO):
                            build_onehots(1, 1, m)
                    elif not (static(p, 0) or last):
                        for m in built_tables(u):
                            build_onehots(p + 1, 1 - par, m)
                    for c in range(GC):
                        if static(p, 0) and (u, c) == (0, 2):
                            split_low(NO + 1)
                            build_onehots(0, 0, NO + 1)
                        copy_gram(p, u, c)
                    if static(p, 0) and u == 0:
                        for m in range(NO + 2, NO + NX):
                            split_low(m)
                            build_onehots(0, 0, m)
                        dve.wait_ge(lo_ready, NO + NX)

            run_pairs(dve, pair)
            pick_pairs(TILES - 1)


def windows(z2, row, n):
    flat = z2[:, :, :].rearrange("p g f -> p (g f)")
    start = row * PITCH + row + 1
    rows = flat[:, start:start + (n - 1) * (PITCH + 1) + HALF]
    return bass.AP(tensor=rows.tensor, offset=rows.offset, ap=[list(rows.ap[0]), [PITCH + 1, n], [1, HALF]])


def kernel(**inputs):
    import concourse.bacc as bacc
    from concourse.bass_utils import run_bass_kernel_spmd as run

    nc = bacc.Bacc("TRN2", target_bir_lowering=False, num_devices=1)
    laid = {
        "dense_t": np.asarray(inputs["r_dense_x"]).T,
        "ids": inputs["ids"],
        "ids_t": np.ascontiguousarray(np.asarray(inputs["ids"]).T[ONEHOT + EXTRA]),
        "w1": np.asarray(inputs["W_top1"])[top1_row_order()],
        "b1": inputs["b_top1"],
        "w2": inputs["W_top2"],
        "b2": inputs["b_top2"],
        "w3": inputs["W_top3"],
    }
    for f in range(26):
        laid[f"tbl_{f}"] = inputs[f"tbl_{f}"]
    arrays, aps = {}, {}
    for name, a in laid.items():
        a = np.ascontiguousarray(a)
        arrays["in_" + name] = a
        aps[name] = nc.dram_tensor("in_" + name, a.shape, mybir.dt.from_np(a.dtype), kind="ExternalInput").ap()
    out = nc.dram_tensor("out_y", (B, 1), F32, kind="ExternalOutput").ap()
    tables = [aps.pop(f"tbl_{f}") for f in range(26)]
    build(nc, out=out, tables=tables, **aps)
    r = run(nc, [arrays], core_ids=[0])
    return r.results[0]["out_y"]
```
